# Optimizing a Trainium2 kernel written in Bass

```python
import numpy as np
import jax
import jax.numpy as jnp

def _softmax(x, axis=-1):
    return jax.nn.softmax(x, axis=axis)

def _gelu(x):
    return jax.nn.gelu(x, approximate=True)

def _silu(x):
    return jax.nn.silu(x)

def _sigmoid(x):
    return jax.nn.sigmoid(x)

def _layernorm(x, axis=-1, eps=1e-05):
    m = jnp.mean(x, axis=axis, keepdims=True)
    v = jnp.var(x, axis=axis, keepdims=True)
    return (x - m) / jnp.sqrt(v + eps)

def _scatter_add(tgt, idx, src, axis=0):
    return tgt.at[idx].add(src)

def _segment_sum(src, seg, n):
    return jax.ops.segment_sum(src, seg, n)
kernel_name = 'mk_adj_preln_d4_adj_r2_e9d646'

def setup_inputs(seed: int=0):
    np.random.seed(seed)
    _w = jnp.asarray

    def _rec_inputs():
        import jax
        import jax.numpy as jnp
        _gk = jax.random.key(seed)
        x = -0.0005207 + 1.001 * jax.random.normal(jax.random.fold_in(_gk, 1), (4096, 128), jnp.float32)
        _w = (1.0 + jnp.arange(4096, dtype=jnp.float32)) ** (-0.5)
        _w = _w / _w.mean()
        _pij = jnp.clip(0.000488281 * _w[:, None] * _w[None, :], 0.0, 1.0)
        _a = jax.random.uniform(jax.random.fold_in(_gk, 2), (4096, 4096)) < _pij
        _a = jnp.logical_or(_a, jnp.eye(4096, dtype=bool))
        _af = _a.astype(jnp.float32)
        _af = _af * jax.random.uniform(jax.random.fold_in(_gk, 3), (4096, 4096), jnp.float32, 0.05, 1)
        adj = _af
        return (x, adj)
    x, adj = _rec_inputs()

    def _L0_gnn_setup():
        import jax, jax.numpy as jnp
        import numpy as np
        IN_DIM = 128
        OUT_DIM = 128
        N = 8192
        key = jax.random.key(seed)
        k_x, k_adj, k_w, k_b = jax.random.split(key, 4)
        x = jax.random.normal(k_x, (N, IN_DIM), dtype=jnp.float32)
        adj = jax.random.uniform(k_adj, (N, N), dtype=jnp.float32)
        bound = 1.0 / np.sqrt(2 * IN_DIM)
        W = jax.random.uniform(k_w, (OUT_DIM, 2 * IN_DIM), dtype=jnp.float32, minval=-bound, maxval=bound)
        b = jax.random.uniform(k_b, (OUT_DIM,), dtype=jnp.float32, minval=-bound, maxval=bound)
        return {'x': x, 'adj': adj, 'W': W, 'b': b}
    _L0_gnn_all = _L0_gnn_setup()
    _L0_gnn_in = {k: v for k, v in _L0_gnn_all.items() if k in ('W', 'b')}
    del _L0_gnn_all

    def _L1_gnn_setup():
        import jax, jax.numpy as jnp
        import numpy as np
        CUTOFF = 0.5
        key = jax.random.key(seed)
        k_z, k_d, k_w, k_mu, k_sg = jax.random.split(key, 5)
        N, D_IN, D_OUT = (4096, 128, 128)
        z = jax.random.normal(k_z, (N, D_IN), dtype=jnp.float32)
        dist_matrix = jax.random.uniform(k_d, (N, N), dtype=jnp.float32)
        W = jax.random.normal(k_w, (D_IN, D_OUT), dtype=jnp.float32)
        B = jnp.zeros((D_OUT,), dtype=jnp.float32)
        mu = jax.random.normal(k_mu, (1,), dtype=jnp.float32)
        sigma = jax.random.normal(k_sg, (1,), dtype=jnp.float32)
        return {'z': z, 'dist_matrix': dist_matrix, 'W': W, 'B': B, 'mu': mu, 'sigma': sigma}
    _L1_gnn_all = _L1_gnn_setup()
    _L1_gnn_in = {k: v for k, v in _L1_gnn_all.items() if k in ('W', 'B', 'mu', 'sigma')}
    del _L1_gnn_all

    def _L2_gnn_setup():
        import jax, jax.numpy as jnp
        import numpy as np
        N, EMB, HID = (4096, 128, 128)
        key = jax.random.key(seed)
        k1, k2, k3, k4, k5, k6, k7, k8 = jax.random.split(key, 8)
        inlayer = jax.random.normal(k1, (N, EMB), dtype=jnp.float32)
        inlayer2 = jax.random.normal(k2, (N, 2 * EMB), dtype=jnp.float32)
        adj_mat = jax.random.randint(k3, (N, N), 0, 2).astype(jnp.float32)
        W1 = jax.random.normal(k4, (HID, 2 * EMB), dtype=jnp.float32) / np.sqrt(2 * EMB)
        w2 = jax.random.normal(k5, (HID,), dtype=jnp.float32) / np.sqrt(HID)
        b2 = jax.random.normal(k6, (), dtype=jnp.float32) * 0.01
        w3 = jax.random.normal(k7, (HID,), dtype=jnp.float32) / np.sqrt(HID)
        b3 = jax.random.normal(k8, (), dtype=jnp.float32) * 0.01
        return {'inlayer': inlayer, 'inlayer2': inlayer2, 'adj_mat': adj_mat, 'W1': W1, 'w2': w2, 'b2': b2, 'w3': w3, 'b3': b3}
    _L2_gnn_all = _L2_gnn_setup()
    _L2_gnn_in = {k: v for k, v in _L2_gnn_all.items() if k in ('inlayer2', 'W1', 'w2', 'b2', 'w3', 'b3')}
    del _L2_gnn_all

    def _L3_gnn_setup():
        import jax, jax.numpy as jnp
        import numpy as np

        def _lap_mul(A, x):
            d = 1.0 / jnp.sqrt(jnp.sum(A, axis=-1))
            return d[:, None] * (A @ (d[:, None] * x))
        key = jax.random.key(seed)
        k1, k2, k3, k4, k5, k6 = jax.random.split(key, 6)
        N, D_IN, D_OUT = (2048, 128, 128)
        x = jax.random.normal(k1, (N, D_IN), dtype=jnp.float32)
        A = jax.random.uniform(k2, (N, N), dtype=jnp.float32)
        s1 = 1.0 / np.sqrt(D_IN)
        W1 = jax.random.uniform(k3, (D_IN, D_OUT), minval=-s1, maxval=s1, dtype=jnp.float32)
        b1 = jax.random.uniform(k4, (D_OUT,), minval=-s1, maxval=s1, dtype=jnp.float32)
        W2 = jax.random.uniform(k5, (D_IN, D_OUT), minval=-s1, maxval=s1, dtype=jnp.float32)
        b2 = jax.random.uniform(k6, (D_OUT,), minval=-s1, maxval=s1, dtype=jnp.float32)
        return {'x': x, 'A': A, 'W1': W1, 'b1': b1, 'W2': W2, 'b2': b2, 'sigma': 1, 'k': 4}
    _L3_gnn_all = _L3_gnn_setup()
    _L3_gnn_in = {k: v for k, v in _L3_gnn_all.items() if k in ('W1', 'b1', 'W2', 'b2')}
    del _L3_gnn_all
    return {'x': x, 'adj': adj, 'L0_gnn_W': _L0_gnn_in['W'], 'L0_gnn_b': _L0_gnn_in['b'], 'L1_gnn_W': _L1_gnn_in['W'], 'L1_gnn_B': _L1_gnn_in['B'], 'L1_gnn_mu': _L1_gnn_in['mu'], 'L1_gnn_sigma': _L1_gnn_in['sigma'], 'L2_gnn_inlayer2': _L2_gnn_in['inlayer2'], 'L2_gnn_W1': _L2_gnn_in['W1'], 'L2_gnn_w2': _L2_gnn_in['w2'], 'L2_gnn_b2': _L2_gnn_in['b2'], 'L2_gnn_w3': _L2_gnn_in['w3'], 'L2_gnn_b3': _L2_gnn_in['b3'], 'L3_gnn_W1': _L3_gnn_in['W1'], 'L3_gnn_b1': _L3_gnn_in['b1'], 'L3_gnn_W2': _L3_gnn_in['W2'], 'L3_gnn_b2': _L3_gnn_in['b2']}

def reference(x, adj, L0_gnn_W, L0_gnn_b, L1_gnn_W, L1_gnn_B, L1_gnn_mu, L1_gnn_sigma, L2_gnn_inlayer2, L2_gnn_W1, L2_gnn_w2, L2_gnn_b2, L2_gnn_w3, L2_gnn_b3, L3_gnn_W1, L3_gnn_b1, L3_gnn_W2, L3_gnn_b2):
    import jax
    import jax.numpy as jnp

    def _L0_gnn_ref(x, adj, W, b):
        import jax, jax.numpy as jnp
        import numpy as np
        IN_DIM = 128
        OUT_DIM = 128
        N = 8192
        h_N = jnp.matmul(adj, x)
        h_cat = jnp.concatenate([x, h_N], axis=-1)
        out = jnp.maximum(jnp.einsum('nd,od->no', h_cat, W) + b, 0.0)
        return out

    def _L1_gnn_ref(z, dist_matrix, W, B, mu, sigma):
        import jax, jax.numpy as jnp
        import numpy as np
        CUTOFF = 0.5
        N = dist_matrix.shape[0]
        h = z @ W + B
        mask = (dist_matrix < CUTOFF) & ~jnp.eye(N, dtype=bool)
        r = jnp.where(mask, dist_matrix, 1.0)
        sens = jnp.exp(-(1.0 / r - 1.0 / mu[0]) ** 2 / (2.0 * sigma[0] ** 2))
        S = jnp.where(mask, sens, 0.0)
        return S @ h

    def _L2_gnn_ref(inlayer, inlayer2, adj_mat, W1, w2, b2, w3, b3):
        import jax, jax.numpy as jnp
        import numpy as np
        N, EMB, HID = (4096, 128, 128)
        in_fts = jnp.einsum('ne,he->nh', inlayer2, W1)
        f1 = in_fts @ w2 + b2
        f2 = in_fts @ w3 + b3
        logits = f1[:, None] + f2[None, :]
        logits = adj_mat * logits
        bias_mat = -1000000000.0 * (1.0 - (adj_mat > 0).astype(jnp.float32))
        coefs = jax.nn.softmax(jax.nn.leaky_relu(logits, 0.01) + bias_mat, axis=1)
        vals = coefs @ inlayer
        return vals

    def _L3_gnn_ref(x, A, W1, b1, W2, b2, sigma, k):
        import jax, jax.numpy as jnp
        import numpy as np

        def _lap_mul(A, x):
            d = 1.0 / jnp.sqrt(jnp.sum(A, axis=-1))
            return d[:, None] * (A @ (d[:, None] * x))
        z = _lap_mul(A, x) @ W1 + b1
        z = jax.nn.leaky_relu(z, negative_slope=0.1)
        sq = jnp.sum(z * z, axis=-1)
        d2 = sq[:, None] + sq[None, :] - 2.0 * (z @ z.T)
        d2 = jnp.maximum(d2, 0.0)
        S = jnp.sqrt(d2 + 1e-10)
        S = jnp.exp(-S / (2.0 * sigma))
        order = jnp.argsort(-S, axis=-1)
        ranks = jnp.argsort(order, axis=-1)
        S = jnp.where(ranks < k, S, 0.0)
        A2 = S + A
        out = _lap_mul(A2, x) @ W2 + b2
        return out
    h = jnp.maximum(_layernorm(x, axis=-1), 0.0)
    x = x + _L0_gnn_ref(h, adj, L0_gnn_W, L0_gnn_b)
    h = jnp.maximum(_layernorm(x, axis=-1), 0.0)
    x = x + _L1_gnn_ref(h, adj, L1_gnn_W, L1_gnn_B, L1_gnn_mu, L1_gnn_sigma)
    h = jnp.maximum(_layernorm(x, axis=-1), 0.0)
    x = x + _L2_gnn_ref(h, L2_gnn_inlayer2, adj, L2_gnn_W1, L2_gnn_w2, L2_gnn_b2, L2_gnn_w3, L2_gnn_b3)
    h = jnp.maximum(_layernorm(x, axis=-1), 0.0)
    x = x + _L3_gnn_ref(h, adj, L3_gnn_W1, L3_gnn_b1, L3_gnn_W2, L3_gnn_b2, 1, 4)
    return x

_drawn_inputs = setup_inputs


def setup_inputs(seed=0):
    import zlib

    import numpy as np

    out = dict(_drawn_inputs(seed))
    spreads = {'L1_gnn_B': (0.0, 0.8)}
    factors = {'L1_gnn_W': 8.0, 'L3_gnn_b1': 3.184}
    for name, (base, spread) in spreads.items():
        noise = np.random.default_rng([zlib.crc32(name.encode()), seed]).standard_normal(out[name].shape)
        drawn = base * np.exp(spread * noise) if base else spread * noise
        out[name] = jnp.asarray(drawn.astype(out[name].dtype))
    for name, factor in factors.items():
        out[name] = (out[name] * factor).astype(out[name].dtype)
    return out
```

```python
from contextlib import ExitStack

import concourse.bass as bass
from concourse import mybir

F32 = mybir.dt.float32
BF16 = mybir.dt.bfloat16
U32 = mybir.dt.uint32
ACT = mybir.ActivationFunctionType
ALU = mybir.AluOpType
AX = mybir.AxisListType

P = 128
N = 4096
NT = N // P
BT = 4
BW = BT * P
NB = N // BW
CT = 4
NC = NT // CT
CW = CT * BW
TOP = 4
EPS = 1e-5
TINY = 2.0 ** -40
BIG = 2.0 ** 30
SLOPE2 = 0.01
SLOPE3 = 0.1


def gnn_kernel(nc, x_in, adj, adjT, w0T, b0, w1, b1, mu, sigma, inlT, wfT, wf1, bf1, wf2, bf2,
               w31, b31, w32, b32, out):
    x_rows = x_in.rearrange("(t p) d -> p t d", p=P)
    out_rows = out.rearrange("(t p) d -> p t d", p=P)
    adjT_v = adjT.rearrange("(t p) i -> p t i", p=P)
    adj_v = adj.rearrange("(t p) j -> p t j", p=P)
    table4_dram = nc.dram_tensor("table4_plain", (N, P), F32, kind="Internal").ap()
    table4s_dram = nc.dram_tensor("table4_scaled", (N, P), F32, kind="Internal").ap()
    table4_rows = table4_dram.rearrange("(t p) d -> p t d", p=P)
    table4s_rows = table4s_dram.rearrange("(t p) d -> p t d", p=P)

    ctx = ExitStack()
    with ctx:
        def sb(name, shape, dt=F32):
            return ctx.enter_context(nc.sbuf_tensor(name, shape, dt))

        def sem(name):
            return ctx.enter_context(nc.semaphore(name))

        X = sb("x_feat", [P, NT, P])
        Ga = sb("table_a", [P, NT, P])
        Gb = sb("table_b", [P, NT, P])
        A = sb("adj_ring", [P, NC, CW])
        Q = sb("work", [P, 16384])
        E = sb("work_small", [P, 2048])
        f2_bc = sb("f2_bc", [P, N])
        yT = sb("y_turned", [P, BW])
        hs = sb("h_stage", [P, BT, P])
        W31 = sb("w31_sb", [P, P])
        W32 = sb("w32_sb", [P, P])
        ident = sb("ident", [P, P])
        sm = sb("small", [P, 256])
        col = sb("columns", [P, 32])
        Gb_flat = Gb[:, :, :].rearrange("p t d -> p (t d)")
        hs_flat = hs[:, :, :].rearrange("p k d -> p (k d)")
        A_flat = A[:, :, :].rearrange("p c w -> p (c w)")

        f1_col, deg, dinv = sm[:, 0:32], sm[:, 32:64], sm[:, 64:96]
        rsum, sq_col, dinv2 = sm[:, 96:128], sm[:, 128:160], sm[:, 160:192]
        st6 = sm[:, 192:216].rearrange("p (k s) -> p k s", s=6)
        mv4 = sm[:, 216:224].rearrange("p (k s) -> p k s", s=2)
        ve4, rstd4, nmr4, rinv4 = sm[:, 224:228], sm[:, 228:232], sm[:, 232:236], sm[:, 236:240]
        mx, nm = sm[:, 240:244], sm[:, 244:248]
        negmx = sm[:, 248:252]
        (b0_c, b31_c, wf1_c, wf2_c, mu_c, sg_c, bf1_c, bf2_c, one_c, mhalf_c, half_c, tiny_c,
         imu_c, sg2_c, nk_c) = (col[:, i:i + 1] for i in range(15))

        W0x, W0n, W1 = E[:, 0:128], E[:, 128:256], E[:, 256:384]
        wf2_rep, b1_bc = E[:, 384:512], E[:, 512:640]
        WfT = E[:, 640:896].rearrange("p (e h) -> p e h", e=2)
        dsum, dpart = E[:, 1024:1536], E[:, 1536:2048]
        pen = E[:, :].bitcast(BF16)
        b32_bc = E[:, 0:128]
        inl = Q[:, 0:8192].rearrange("p (e n) -> p e n", e=2)
        ft = Q[:, 8192:8704]
        ht0 = [Q[:, 8704:9216], Q[:, 9216:9728]]
        hs0 = [Q[:, 9728:10240].rearrange("p (k d) -> p k d", d=P),
               Q[:, 10240:10752].rearrange("p (k d) -> p k d", d=P)]
        st0 = Q[:, 10752:10944].rearrange("p (t s) -> p t s", s=6)
        mean0, var0, rstd0, nmr0, tmp0 = (Q[:, 10944 + 32 * i:10976 + 32 * i] for i in range(5))
        PT = [Q[:, 8192 * h:8192 * (h + 1)].rearrange("p (t i) -> p t i", t=NT) for h in range(2)]
        zT = Q[:, 0:4096]
        sq_parts = Q[:, 4096:6144].bitcast(BF16)
        keys = [Q[:, 6144:10240], Q[:, 10240:14336]]
        ones = Q[:, 14336:14464]
        pick = Q[:, 14464:14528].bitcast(BF16)
        z_st = [Q[:, 14528:14656], Q[:, 14656:14784]]
        dg = Q[:, 14784:15296].rearrange("p (k d) -> p k d", d=P)
        zz = Q[:, 15296:15808]
        kval = Q[:, 15808:16064].rearrange("p (t s) -> p t s", s=8)
        kidx = Q[:, 16064:16320].bitcast(U32).rearrange("p (t s) -> p t s", s=8)
        p1f = Q[:, 6144:6400].bitcast(BF16)
        p2f = Q[:, 6400:6656].bitcast(BF16)
        s2f, s3f = Q[:, 6656:7168], Q[:, 7168:7680]
        zb = Q[:, 7680:8192]
        gsum = Q[:, 6144:10240].rearrange("p (t d) -> p t d", d=P)
        gath = [Q[:, 10240 + 512 * u:10752 + 512 * u].rearrange("p (k d) -> p k d", d=P) for u in range(2)]
        S4 = Q[:, 11264:11392].rearrange("p (t k) -> p t k", k=TOP)
        dist = Q[:, 11392:11520].rearrange("p (t k) -> p t k", k=TOP)
        s4sum = Q[:, 11520:11552]
        v8 = [sm[:, 192:200], sm[:, 200:208]]
        i8 = [sm[:, 208:216].bitcast(U32), sm[:, 216:224].bitcast(U32)]
        idx_st = [sm[:, 224:228].bitcast(U32), sm[:, 228:232].bitcast(U32)]

        ps = ctx.enter_context(nc.psum_tensor("ps", [P, 4096], F32))

        def bank(i, n=1):
            return ps[:, 512 * i:512 * (i + n)]

        def acc(b, off=0, w=BW):
            return ps[:, bass.ds((b % 2) * BW + off, w)]

        epi, epi2 = bank(2), bank(7)
        epi_k = epi.rearrange("p (k d) -> p k d", d=P)
        epi2_k = epi2.rearrange("p (k d) -> p k d", d=P)
        turn = [bank(3, 2).rearrange("p (t i) -> p t i", i=P), bank(5, 2).rearrange("p (t i) -> p t i", i=P)]

        def rows(T, b):
            return T[:, bass.ds(b * BT, BT), :]

        def block_cols(T, b):
            return T[:, bass.ds(b * BW, BW)]

        par_in, x_ld, inl_in, w3_in, b32_in = (sem(n) for n in ("par_in", "x_ld", "inl_in", "w3_in", "b32_in"))
        consts = sem("consts")
        dconst = sem("dconst")
        chunk_in = [sem(f"chunk_in{c}") for c in range(NC)]
        row_in = [sem(f"row_in{s}") for s in range(4)]
        s_bn, s_stat, s_rstd, s_pool = sem("s_bn"), sem("s_stat"), sem("s_rstd"), sem("s_pool")
        s_h, s_turned, s_ht, s_keep, s_gmm, s_g = (sem(n) for n in ("s_h", "s_turned", "s_ht", "s_keep", "s_gmm", "s_g"))
        s_f1mm, s_ft, s_f2mm, s_f = sem("s_f1mm"), sem("s_ft"), sem("s_f2mm"), sem("s_f")
        used = [sem(f"used{i}") for i in range(5)]
        acc_copied = [sem(f"acc_copied{i}") for i in range(5)]
        y_rows = [sem(f"y_rows{i}") for i in range(5)]
        x_new = [sem(f"x_new{i}") for i in range(3)]
        bn_done = [sem(f"bn_done{i}") for i in range(3)]
        stats = [sem(f"stats{i}") for i in range(3)]
        pool_ch = [sem(f"pool_ch{i}") for i in range(3)]
        rstd_ok = [sem(f"rstd_ok{i}") for i in range(3)]
        h_rows = [sem(f"h_rows{i}") for i in range(3)]
        h_turned = [sem(f"h_turned{i}") for i in range(3)]
        ht_copied = [sem(f"ht_copied{i}") for i in range(3)]
        g_mm = [sem(f"g_mm{i}") for i in range(3)]
        g_ok = [sem(f"g_ok{i}") for i in range(3)]
        deg_part, deg_sum, deg_mm, deg_ok, dinv_ok = (sem(n) for n in ("deg_part", "deg_sum", "deg_mm", "deg_ok", "dinv_ok"))
        q_root, q_sq, e_ok, y_ok, z_sq, s_exp, s_mask, s_diag = (
            sem(n) for n in ("q_root", "q_sq", "e_ok", "y_ok", "z_sq", "s_exp", "s_mask", "s_diag"))
        pen_ok, t_ok, mx_ok, nm_a, nm_ok, l_ok, p_ok = (
            sem(n) for n in ("pen_ok", "t_ok", "mx_ok", "nm_a", "nm_ok", "l_ok", "p_ok"))
        p_turned, pt_ok, m_done, rinv_ok = (sem(n) for n in ("p_turned", "pt_ok", "m_done", "rinv_ok"))
        g4_st, g4_out, g4_in = sem("g4_st"), sem("g4_out"), sem("g4_in")
        l3_const, dg_ok, dbc_mm, dbc_ok, zs_ok, zb_ok, z_ok, zz_ok, sq_mm, sqc_ok, sq_half, sp_ch, sp_ok = (
            sem(n) for n in ("l3_const", "dg_ok", "dbc_mm", "dbc_ok", "zs_ok", "zb_ok", "z_ok", "zz_ok",
                             "sq_mm", "sqc_ok", "sq_half", "sp_ch", "sp_ok"))
        zst_ok, key_mm, key_ok, v8_ok, i8_ok, top_ok, xb_ok = (
            sem(n) for n in ("zst_ok", "key_mm", "key_ok", "v8_ok", "i8_ok", "top_ok", "xb_ok"))
        d_ch, d_pool, s4_ok, d2_sum, d2_ok, g4s_ok, g4s_out = (
            sem(n) for n in ("d_ch", "d_pool", "s4_ok", "d2_sum", "d2_ok", "g4s_ok", "g4s_out"))
        idx_ok, gath_in, gs_ch, gs_ok = sem("idx_ok"), [sem("gath_in0"), sem("gath_in1")], sem("gs_ch"), sem("gs_ok")
        o_sum, o_ok, o_out = sem("o_sum"), sem("o_ok"), sem("o_out")

        block = ctx.enter_context(nc.Block())

        passed = sem("passed")

        def hold(eng, *waits):
            for semaphore, value in waits:
                eng.wait_ge(semaphore, value)
                eng.sem_inc(passed, 1)

        @block.sync
        def _(sp):
            sp.dma_start(X[:, :, :], x_rows).then_inc(x_ld, 16)
            for dst, src in ((W0x, w0T[0:P, :]), (W0n, w0T[P:2 * P, :]), (W1, w1),
                             (WfT, wfT.rearrange("(e p) h -> p e h", p=P)),
                             (b1_bc, b1.partition_broadcast(P)),
                             (b0_c, b0.unsqueeze(1)), (b31_c, b31.unsqueeze(1)),
                             (wf1_c, wf1.unsqueeze(1)), (wf2_c, wf2.unsqueeze(1)),
                             (mu_c, mu.partition_broadcast(P)), (sg_c, sigma.partition_broadcast(P)),
                             (bf1_c, bf1.partition_broadcast(P)), (bf2_c, bf2.partition_broadcast(P)),
                             (W31[:, :], w31), (W32[:, :], w32)):
                sp.dma_start(dst, src).then_inc(par_in, 16)
            sp.dma_start(inl, inlT.rearrange("(e p) n -> p e n", p=P)).then_inc(inl_in, 16)

            def load_chunk(b, c):
                sp.dma_start(A[:, c, :].rearrange("p (t i) -> p t i", t=CT),
                             adjT_v[:, CT * c:CT * (c + 1), bass.ds(b * BW, BW)]).then_inc(chunk_in[c], 16)

            for c in range(NC):
                load_chunk(0, c)
            with sp.Fori(1, NB) as b:
                for c in range(NC):
                    hold(sp, (used[0], b * NC + (c + 1 - NC)), (deg_part, b * (NC // 2) + (c // 2 + 1 - NC // 2)))
                    load_chunk(b, c)
            for c in range(NC):
                sp.wait_ge(used[0], NC * (NB - 1) + c + 1)
                sp.wait_ge(deg_part, (NC // 2) * (NB - 1) + c // 2 + 1)
                load_chunk(0, c)
            with sp.Fori(1, NB) as b:
                for c in range(NC):
                    sp.wait_ge(s_mask, b * NC + (c + 1 - NC))
                    load_chunk(b, c)

            def load_row(r, s):
                sp.dma_start(A_flat[:, N * s:N * (s + 1)], adj_v[:, bass.ds(r, 1), :].rearrange("p t j -> p (t j)")).then_inc(row_in[s], 16)

            for s in range(BT):
                sp.wait_ge(s_mask, NC * (NB - 1) + 2 * s + 2)
                load_row(s, s)
            with sp.Fori(1, NB) as g:
                for s in range(BT):
                    sp.wait_ge(p_turned, g * (4 * BT) + (4 * (s + 1) - 4 * BT))
                    load_row(g * BT + s, s)
            for c in range(NC):
                sp.wait_ge(p_turned, 4 * (NT - BT + c // 2 + 1))
                load_chunk(0, c)
            with sp.Fori(1, NB) as b:
                for c in range(NC):
                    sp.wait_ge(used[3], b * NC + (c + 1 - NC))
                    load_chunk(b, c)
            for c in range(NC):
                sp.wait_ge(used[3], NC * (NB - 1) + c + 1)
                load_chunk(0, c)
            with sp.Fori(1, NB) as b:
                for c in range(NC):
                    sp.wait_ge(used[4], b * NC + (c + 1 - NC))
                    load_chunk(b, c)

        @block.tensor
        def _(pe):
            pe.wait_ge(consts, 3)
            pe.wait_ge(par_in, 15 * 16)
            pe.wait_ge(dconst, 1)
            pe.wait_ge(inl_in, 16)
            with pe.Fori(0, NB // 2) as i:
                for u in range(2):
                    b = 2 * i + u
                    pe.wait_ge(s_ft, b)
                    for e in range(2):
                        mm = nc.tensor.matmul(bank(6), WfT[:, e, :], block_cols(inl[:, e, :], b),
                                              start=e == 0, stop=e == 1)
                    mm.then_inc(s_f1mm, 1)
                    pe.wait_ge(s_h, b + 1)
                    pe.wait_ge(s_ht, 2 * i)
                    for k in range(BT):
                        mm = nc.tensor.transpose(bank(2 + u)[:, k * P:(k + 1) * P], hs0[u][:, k, :], ident[:, :])
                    mm.then_inc(s_turned, 1)
                    pe.wait_ge(s_ft, b + 1)
                    pe.wait_ge(s_f, b)
                    nc.tensor.matmul(bank(7), wf2_rep, ft, start=True, stop=True)
                    for k in range(BT):
                        mm = nc.tensor.matmul(bank(0)[:, k:k + 1], ft[:, k * P:(k + 1) * P], wf1_c,
                                              start=True, stop=True)
                    mm.then_inc(s_f2mm, 1)
                    pe.wait_ge(s_ht, b + 1)
                    pe.wait_ge(s_g, 2 * i)
                    for k in range(BT):
                        mm = nc.tensor.matmul(bank(4 + u)[:, k * P:(k + 1) * P], ht0[u][:, k * P:(k + 1) * P],
                                              W0n, start=True, stop=True)
                    mm.then_inc(s_gmm, 1)

            def stream(b, L, G, src, wait_chunk, hooks, wait_table=None):
                if -1 in hooks:
                    hooks[-1]()
                if not isinstance(b, int):
                    pe.wait_ge(acc_copied[L], b - 1)
                if L == 0:
                    nc.tensor.matmul(acc(b), W0x, block_cols(Gb_flat, b), start=True, stop=False)
                for c in range(NC):
                    wait_chunk(b, c)
                    if wait_table is not None:
                        pe.wait_ge(wait_table, c + 1)
                    for k in range(CT):
                        mm = nc.tensor.matmul(acc(b), G[:, CT * c + k, :], src(c, k),
                                              start=(c == 0 and k == 0 and L != 0),
                                              stop=(c == NC - 1 and k == CT - 1))
                    mm.then_inc(used[L], 1)
                    if c in hooks:
                        hooks[c]()

            def landed(before):
                return lambda b, c: pe.wait_ge(chunk_in[c], b * 16 + 16 * (before + 1))

            def slot(c, k):
                return A[:, c, k * BW:(k + 1) * BW]

            def turn_result(L, b):
                pe.wait_ge(acc_copied[L], b + 1)
                for k in range(BT):
                    mm = nc.tensor.transpose(epi[:, k * P:(k + 1) * P], yT[:, k * P:(k + 1) * P], ident[:, :])
                mm.then_inc(y_rows[L], 1)

            def turn_rows(L, b):
                pe.wait_ge(h_rows[L], b + 1)
                for k in range(BT):
                    mm = nc.tensor.transpose(epi[:, k * P:(k + 1) * P], hs[:, k, :], ident[:, :])
                mm.then_inc(h_turned[L], 1)

            def next_table(L, b, weights):
                pe.wait_ge(ht_copied[L], b + 1)
                for dst, w in weights:
                    for k in range(BT):
                        mm = nc.tensor.matmul(dst[:, k * P:(k + 1) * P], yT[:, k * P:(k + 1) * P], w,
                                              start=True, stop=True)
                mm.then_inc(g_mm[L], 1)

            def degrees(b):
                pe.wait_ge(deg_sum, b * 3 + 3)
                for k in range(BT):
                    mm = nc.tensor.matmul(epi2[:, k:k + 1], dsum[:, k * P:(k + 1) * P], one_c,
                                          start=True, stop=True)
                mm.then_inc(deg_mm, 1)

            def epilogue0(b):
                def t1():
                    pe.wait_ge(g_ok[0], b)
                    turn_result(0, b)
                return {0: lambda: degrees(b), 1: t1, 3: lambda: turn_rows(0, b),
                        5: lambda: next_table(0, b, [(epi, W1)])}

            pe.wait_ge(s_keep, NB)
            pe.wait_ge(s_f, NB)
            pe.wait_ge(s_g, NB)
            stream(0, 0, Ga, slot, landed(0), {})
            with pe.Fori(1, NB) as b:
                stream(b, 0, Ga, slot, landed(0), epilogue0(b - 1))
            for _, hook in sorted(epilogue0(NB - 1).items()):
                hook()

            def epilogue1(b):
                def t1():
                    pe.wait_ge(x_new[1], b)
                    turn_result(1, b)
                return {-1: t1}

            def masked(c, k):
                return Q[:, CW * c + k * BW:CW * c + (k + 1) * BW]

            def mask_on(b, c):
                pe.wait_ge(s_mask, b * NC + (c + 1))

            pe.wait_ge(g_ok[0], NB)
            stream(0, 1, Gb, masked, mask_on, {})
            with pe.Fori(1, NB) as b:
                stream(b, 1, Gb, masked, mask_on, epilogue1(b - 1))
            epilogue1(NB - 1)[-1]()

            def turn_weights(r, s):
                pe.wait_ge(p_ok, r + 1)
                for q in range(4):
                    if not (isinstance(r, int) and 4 * r + q < 2):
                        pe.wait_ge(pt_ok, r * 4 + (q - 1))
                    for t in range(8):
                        j = 8 * q + t
                        mm = nc.tensor.transpose(turn[q % 2][:, t, :], A_flat[:, N * s + j * P:N * s + (j + 1) * P],
                                                 ident[:, :])
                    mm.then_inc(p_turned, 1)

            def half_block(g, h):
                pe.wait_ge(pt_ok, g * (4 * BT) + 8 * (h + 1))
                for j in range(NT):
                    mm = nc.tensor.matmul(acc(g, h * 256, 256), Ga[:, j, :], PT[h][:, j, :],
                                          start=j == 0, stop=j == NT - 1)
                mm.then_inc(m_done, 1)

            def t1_attention(b):
                pe.wait_ge(g_ok[2], b)
                turn_result(2, b)

            def last_tables(b):
                pe.wait_ge(g4_st, b)
                next_table(2, b, [(epi, W31[:, :]), (epi2, W32[:, :])])

            pe.wait_ge(x_new[1], NB)
            pe.wait_ge(h_rows[1], NB)
            for s in range(3):
                turn_weights(s, s)
            half_block(0, 0)
            turn_weights(3, 3)
            with pe.Fori(1, NB) as g:
                turn_weights(g * BT, 0)
                half_block(g - 1, 1)
                turn_weights(g * BT + 1, 1)
                t1_attention(g - 1)
                turn_weights(g * BT + 2, 2)
                turn_rows(2, g - 1)
                pe.wait_ge(acc_copied[2], g - 1)
                half_block(g, 0)
                last_tables(g - 1)
                turn_weights(g * BT + 3, 3)
            half_block(NB - 1, 1)
            t1_attention(NB - 1)
            turn_rows(2, NB - 1)
            last_tables(NB - 1)

            pe.wait_ge(l3_const, 4)

            def spread_d(b):
                pe.wait_ge(dg_ok, b + 1)
                pe.wait_ge(sq_half, b)
                for k in range(BT):
                    mm = nc.tensor.matmul(epi[:, k * P:(k + 1) * P], ones, dg[:, k, :], start=True, stop=True)
                mm.then_inc(dbc_mm, 1)

            def squares(b):
                pe.wait_ge(zz_ok, b + 1)
                nc.tensor.matmul(epi, ones, zz, start=True, stop=True)
                pe.wait_ge(sqc_ok, b)
                for k in range(BT):
                    mm = nc.tensor.matmul(epi2[:, k:k + 1], zz[:, k * P:(k + 1) * P], one_c, start=True, stop=True)
                mm.then_inc(sq_mm, 1)

            pe.wait_ge(g_ok[2], NB)
            pe.wait_ge(g4_st, NB)
            stream(0, 3, Gb, slot, landed(2 * NB), {})
            with pe.Fori(1, NB) as b:
                stream(b, 3, Gb, slot, landed(2 * NB),
                       {1: lambda: spread_d(b - 1), 4: lambda: squares(b - 1)})
            spread_d(NB - 1)
            squares(NB - 1)

            pe.wait_ge(z_ok, NB)
            pe.wait_ge(sp_ok, NB)
            pe.wait_ge(sqc_ok, NB)

            def keys_of(r, u):
                pe.wait_ge(zst_ok, r + 1)
                for h in range(2):
                    if not (isinstance(r, int) and r == 0):
                        pe.wait_ge(key_ok, 2 * r + (h - 1))
                    for j in range(4 * h, 4 * h + 4):
                        nc.tensor.matmul(bank(j), z_st[u], zT[:, j * BW:(j + 1) * BW], start=True, stop=False)
                        mm = nc.tensor.matmul(bank(j), pick, sq_parts[:, j * BW:(j + 1) * BW],
                                              start=False, stop=True)
                    mm.then_inc(key_mm, 1)

            keys_of(0, 0)
            with pe.Fori(0, NT // 2 - 1) as i:
                keys_of(2 * i + 1, 1)
                keys_of(2 * i + 2, 0)
            keys_of(NT - 1, 1)

            def turn_last(b):
                pe.wait_ge(o_sum, b)
                turn_result(4, b)

            pe.wait_ge(key_ok, 2 * NT)
            stream(0, 4, Ga, slot, landed(3 * NB), {}, wait_table=g4s_ok)
            with pe.Fori(1, NB) as b:
                stream(b, 4, Ga, slot, landed(3 * NB), {1: lambda: turn_last(b - 1)})
            turn_last(NB - 1)

        @block.scalar
        def _(act):
            act.wait_ge(consts, 3)
            act.wait_ge(par_in, 15 * 16)
            act.wait_ge(s_rstd, 1)
            with act.Fori(0, NB // 2) as i:
                for u in range(2):
                    b = 2 * i + u
                    act.wait_ge(s_f1mm, b + 1)
                    act.wait_ge(s_f2mm, b)
                    nc.scalar.activation(ft, bank(6), ACT.Copy).then_inc(s_ft, 1)
                    hold(act, (s_turned, 2 * i))
                    for k in range(BT):
                        t = bass.ds(b * BT + k, 1)
                        op = nc.scalar.activation(hs0[u][:, k, :], X[:, t, :], ACT.Relu,
                                                  scale=rstd0[:, t], bias=nmr0[:, t])
                    op.then_inc(s_h, 1)
                    act.wait_ge(s_turned, b + 1)
                    act.wait_ge(s_gmm, 2 * i)
                    act.wait_ge(s_keep, 2 * i)
                    nc.scalar.activation(ht0[u], bank(2 + u), ACT.Copy).then_inc(s_ht, 1)

            def normal_rows(L, b, dst, free=()):
                hold(act, *free, (rstd_ok[L], b + 1))
                for k in range(BT):
                    op = nc.scalar.activation(dst(b, k), X[:, bass.ds(b * BT + k, 1), :], ACT.Relu,
                                              scale=rstd4[:, k:k + 1], bias=nmr4[:, k:k + 1])
                op.then_inc(h_rows[L], 1)

            def stage(b, k):
                return hs[:, k:k + 1, :]

            def table_a(b, k):
                return Ga[:, bass.ds(b * BT + k, 1), :]

            def copy_turned(L, b):
                act.wait_ge(h_turned[L], b + 1)
                nc.scalar.activation(yT[:, :], epi, ACT.Copy).then_inc(ht_copied[L], 1)

            with act.Fori(0, NB) as b:
                hold(act, (used[0], b * NC + NC), (g_mm[0], b))
                nc.scalar.activation(yT[:, :], acc(b), ACT.Relu, bias=b0_c).then_inc(acc_copied[0], 1)
                normal_rows(0, b, stage, [(h_turned[0], b)])
                copy_turned(0, b)

            W2 = 2 * CW

            def roots(b, m):
                for j in (2 * m, 2 * m + 1):
                    for c in (2 * j, 2 * j + 1):
                        act.wait_ge(chunk_in[c], b * 16 + 16 * (NB + 1))
                    if not isinstance(b, int):
                        act.wait_ge(used[1], b * NC + (2 * j + 2 - NC))
                    nc.scalar.activation(Q[:, W2 * j:W2 * (j + 1)], A_flat[:, W2 * j:W2 * (j + 1)],
                                         ACT.Abs_reciprocal_sqrt, bias=tiny_c).then_inc(q_root, 1)
                for j in (2 * m, 2 * m + 1):
                    act.wait_ge(q_root, b * 4 + (j + 1))
                    nc.scalar.activation(Q[:, W2 * j:W2 * (j + 1)], Q[:, W2 * j:W2 * (j + 1)],
                                         ACT.Square).then_inc(q_sq, 1)

            def kernels(b, m):
                for j in (2 * m, 2 * m + 1):
                    act.wait_ge(y_ok, b * NC + (2 * j + 2))
                    nc.scalar.activation(Q[:, W2 * j:W2 * (j + 1)], Q[:, W2 * j:W2 * (j + 1)],
                                         ACT.Square, bias=imu_c).then_inc(z_sq, 1)
                for j in (2 * m, 2 * m + 1):
                    act.wait_ge(z_sq, b * 4 + (j + 1))
                    nc.scalar.activation(Q[:, W2 * j:W2 * (j + 1)], Q[:, W2 * j:W2 * (j + 1)],
                                         ACT.Exp, scale=nk_c).then_inc(s_exp, 1)

            act.wait_ge(dconst, 5)
            roots(0, 0)
            roots(0, 1)
            kernels(0, 0)
            with act.Fori(1, NB) as b:
                roots(b, 0)
                kernels(b - 1, 1)
                roots(b, 1)
                kernels(b, 0)
                normal_rows(1, b - 1, table_a)
            kernels(NB - 1, 1)
            normal_rows(1, NB - 1, table_a)

            def weights(g, s):
                r = g * BT + s
                hold(act, (l_ok, r + 1))
                row = A_flat[:, N * s:N * (s + 1)]
                nc.scalar.activation(row, row, ACT.Exp, bias=nm[:, s:s + 1],
                                     accum_out=rsum[:, bass.ds(r, 1)]).then_inc(p_ok, 1)

            def copy_weights(g, s):
                r, h = g * BT + s, s // 2
                if not isinstance(g, int):
                    act.wait_ge(m_done, g * 2 + (h - 1))
                for q in range(4):
                    act.wait_ge(p_turned, r * 4 + (q + 1))
                    nc.scalar.activation(PT[h][:, 8 * q:8 * (q + 1), (s % 2) * P:(s % 2 + 1) * P],
                                         turn[q % 2], ACT.Copy).then_inc(pt_ok, 1)

            def copy_result(b):
                hold(act, (m_done, b * 2 + 2), (g_mm[2], b))
                nc.scalar.activation(yT[:, :], acc(b), ACT.Copy).then_inc(acc_copied[2], 1)

            def normal_rows2(b):
                normal_rows(2, b, stage, [(g4_out, b * 16)])

            def table3(b):
                hold(act, (g_mm[2], b + 1))
                for k in range(BT):
                    t = bass.ds(b * BT + k, 1)
                    op = nc.scalar.activation(Gb[:, t, :], epi_k[:, k:k + 1, :], ACT.Copy, scale=dinv[:, t])
                op.then_inc(g_ok[2], 1)

            act.wait_ge(dinv_ok, 1)
            weights(0, 0)
            for s in range(1, BT):
                weights(0, s)
                copy_weights(0, s - 1)
            with act.Fori(1, NB) as g:
                weights(g, 0)
                act.wait_ge(m_done, (g - 1) * 2)
                copy_last = g - 1
                for q in range(4):
                    act.wait_ge(p_turned, copy_last * (4 * BT) + (4 * (BT - 1) + q + 1))
                    nc.scalar.activation(PT[1][:, 8 * q:8 * (q + 1), P:2 * P], turn[q % 2],
                                         ACT.Copy).then_inc(pt_ok, 1)
                weights(g, 1)
                copy_weights(g, 0)
                copy_result(g - 1)
                weights(g, 2)
                copy_weights(g, 1)
                normal_rows2(g - 1)
                weights(g, 3)
                copy_weights(g, 2)
                copy_turned(2, g - 1)
                table3(g - 1)
            copy_weights(NB - 1, BT - 1)
            copy_result(NB - 1)
            normal_rows2(NB - 1)
            copy_turned(2, NB - 1)
            table3(NB - 1)

            act.wait_ge(g4_out, 16 * NB)
            with act.Fori(0, NB) as b:
                act.wait_ge(dbc_mm, b + 1)
                act.wait_ge(acc_copied[3], b)
                nc.scalar.activation(hs_flat, epi, ACT.Copy).then_inc(dbc_ok, 1)
                act.wait_ge(acc_copied[3], b + 1)
                nc.scalar.activation(zb, yT[:, :], ACT.Identity, bias=b31_c).then_inc(zb_ok, 1)
                act.wait_ge(sq_mm, b + 1)
                nc.scalar.activation(yT[:, :], epi, ACT.Copy, scale=-0.5).then_inc(sq_half, 1)

            act.wait_ge(sp_ok, NB)

            def copy_keys(r, u):
                if not isinstance(r, int):
                    act.wait_ge(i8_ok, r - 1)
                for h in range(2):
                    act.wait_ge(key_mm, 2 * r + (h + 1))
                    nc.scalar.activation(keys[u][:, 2048 * h:2048 * (h + 1)], bank(4 * h, 4),
                                         ACT.Copy).then_inc(key_ok, 1)

            copy_keys(0, 0)
            copy_keys(1, 1)
            with act.Fori(1, NT // 2) as i:
                copy_keys(2 * i, 0)
                copy_keys(2 * i + 1, 1)
            act.wait_ge(d_pool, 1)
            nc.scalar.activation(S4, dist, ACT.Exp, scale=-0.5).then_inc(s4_ok, 1)

            def copy_last_result(b):
                hold(act, (used[4], b * NC + NC), (y_rows[4], b))
                nc.scalar.activation(yT[:, :], acc(b), ACT.Copy).then_inc(acc_copied[4], 1)

            def rows_out(b):
                act.wait_ge(o_ok, b + 1)
                act.dma_start(out_rows[:, bass.ds(b * BT, BT), :], rows(X, b)).then_inc(o_out, 16)

            copy_last_result(0)
            with act.Fori(1, NB) as b:
                copy_last_result(b)
                rows_out(b - 1)
            rows_out(NB - 1)
            act.wait_ge(o_out, 16 * NB)

        @block.vector
        def _(dve):
            dve.wait_ge(consts, 3)
            dve.wait_ge(par_in, 15 * 16)
            nc.vector.tensor_scalar(wf2_rep, ident[:, :], 0.0, wf2_c, ALU.mult, ALU.add).then_inc(dconst, 1)
            nc.vector.reciprocal(imu_c, mu_c).then_inc(dconst, 1)
            nc.vector.tensor_tensor(sg2_c, sg_c, sg_c, ALU.mult).then_inc(dconst, 1)
            dve.wait_ge(dconst, 3)
            nc.vector.tensor_scalar(sg2_c, sg2_c, -2.0, None, ALU.mult).then_inc(dconst, 1)
            dve.wait_ge(dconst, 4)
            nc.vector.reciprocal(nk_c, sg2_c).then_inc(dconst, 1)
            dve.wait_ge(x_ld, 16)
            with dve.Fori(0, NB) as b:
                for k in range(BT):
                    t = bass.ds(b * BT + k, 1)
                    op = nc.vector.bn_stats(st0[:, t, :], X[:, t, :])
                op.then_inc(s_bn, 1)
            dve.wait_ge(s_bn, NB)
            nc.vector.tensor_tensor(mean0, st0[:, :, 1], st0[:, :, 4], ALU.add).then_inc(s_stat, 1)
            nc.vector.tensor_tensor(tmp0, st0[:, :, 1], st0[:, :, 4], ALU.subtract).then_inc(s_stat, 1)
            nc.vector.tensor_tensor(var0, st0[:, :, 2], st0[:, :, 5], ALU.add).then_inc(s_stat, 1)
            dve.wait_ge(s_stat, 3)
            nc.vector.tensor_scalar(mean0, mean0, 0.5, None, ALU.mult).then_inc(s_stat, 1)
            nc.vector.scalar_tensor_tensor(tmp0, tmp0, 0.25, tmp0, ALU.mult, ALU.mult).then_inc(s_stat, 1)
            dve.wait_ge(s_stat, 5)
            nc.vector.scalar_tensor_tensor(var0, var0, 1.0 / P, tmp0, ALU.mult, ALU.add).then_inc(s_stat, 1)
            with dve.Fori(0, NB // 2) as i:
                for u in range(2):
                    b = 2 * i + u
                    dve.wait_ge(s_f2mm, b + 1)
                    nc.vector.tensor_scalar(block_cols(f2_bc, b), bank(7), bf2_c, None, ALU.add)
                    nc.vector.tensor_scalar(f1_col[:, bass.ds(b * BT, BT)], bank(0)[:, 0:BT], bf1_c, None,
                                            ALU.add).then_inc(s_f, 1)
                    hold(dve, (s_ht, b + 1))
                    nc.vector.tensor_copy(block_cols(Gb_flat, b), ht0[u]).then_inc(s_keep, 1)
                    hold(dve, (s_gmm, b + 1))
                    nc.vector.tensor_copy(block_cols(Ga[:, :, :].rearrange("p t d -> p (t d)"), b),
                                          bank(4 + u)).then_inc(s_g, 1)

            def row_stats(L, b):
                hold(dve, (x_new[L], b + 1))
                for k in range(BT):
                    op = nc.vector.bn_stats(st6[:, k, :], X[:, bass.ds(b * BT + k, 1), :])
                op.then_inc(bn_done[L], 1)
                hold(dve, (h_rows[L], b), (bn_done[L], b + 1))
                for k in range(BT):
                    op = nc.vector.bn_aggr(mv4[:, k, :], st6[:, k, :])
                op.then_inc(stats[L], 1)

            def add_rows(L, b):
                dve.wait_ge(y_rows[L], b + 1)
                nc.vector.tensor_tensor(rows(X, b), epi_k, rows(X, b), ALU.add).then_inc(x_new[L], 1)

            def degree_part(b, j):
                for c in (2 * j, 2 * j + 1):
                    dve.wait_ge(chunk_in[c], b * 16 + 16)
                if j == 0:
                    dve.wait_ge(deg_mm, b)
                else:
                    dve.wait_ge(deg_sum, b * 3 + (j - 1))
                pair = A_flat[:, 2 * CW * j:2 * CW * (j + 1)].rearrange("p (t i) -> p i t", i=BW)
                nc.vector.tensor_reduce(dsum if j == 0 else dpart, pair, AX.X, ALU.add).then_inc(deg_part, 1)
                if j:
                    dve.wait_ge(deg_part, b * 4 + (j + 1))
                    nc.vector.tensor_tensor(dsum, dsum, dpart, ALU.add).then_inc(deg_sum, 1)

            def degree_out(b):
                hold(dve, (deg_mm, b + 1))
                nc.vector.tensor_copy(deg[:, bass.ds(b * BT, BT)], epi2[:, 0:BT]).then_inc(deg_ok, 1)

            def table1(b):
                dve.wait_ge(g_mm[0], b + 1)
                nc.vector.tensor_tensor(rows(Gb, b), epi_k, b1_bc.unsqueeze(1).broadcast_to([P, BT, P]),
                                        ALU.add).then_inc(g_ok[0], 1)

            for j in range(4):
                degree_part(0, j)
            with dve.Fori(1, NB) as b:
                degree_out(b - 1)
                degree_part(b, 0)
                degree_part(b, 1)
                add_rows(0, b - 1)
                row_stats(0, b - 1)
                degree_part(b, 2)
                degree_part(b, 3)
                table1(b - 1)
            degree_out(NB - 1)
            add_rows(0, NB - 1)
            row_stats(0, NB - 1)
            table1(NB - 1)

            def newton(b, m):
                for c in range(4 * m, 4 * m + 4):
                    q = Q[:, CW * c:CW * (c + 1)]
                    dve.wait_ge(q_sq, b * 4 + (c // 2 + 1))
                    dve.wait_ge(y_ok, b * NC + c)
                    nc.vector.tensor_tensor(E[:, :], A[:, c, :], q, ALU.mult).then_inc(e_ok, 1)
                    dve.wait_ge(e_ok, b * NC + (c + 1))
                    nc.vector.scalar_tensor_tensor(q, E[:, :], 2.0, q, ALU.subtract, ALU.mult).then_inc(y_ok, 1)

            def mask(b, m):
                for c in range(4 * m, 4 * m + 4):
                    q = Q[:, CW * c:CW * (c + 1)]

                    def clear_diagonal():
                        for k in range(CT):
                            d = q[:, k * (BW + P):k * (BW + P) + P]
                            op = nc.vector.scalar_tensor_tensor(d, ident[:, :], 0.0, d, ALU.is_equal, ALU.mult)
                        op.then_inc(s_diag, 1)
                        hold(dve, (s_diag, b + 1))

                    hold(dve, (s_exp, b * 4 + (c // 2 + 1)))

                    if isinstance(b, int):
                        if b == c:
                            clear_diagonal()
                    else:
                        with dve.If((b + (2 * NC - c)) % NC):
                            pass
                        with dve.Else():
                            clear_diagonal()
                    nc.vector.scalar_tensor_tensor(q, A[:, c, :], 0.5, q, ALU.is_lt, ALU.mult).then_inc(s_mask, 1)

            def end_block1(b):
                hold(dve, (used[1], b * NC + NC), (y_rows[1], b))
                nc.vector.tensor_copy(yT[:, :], acc(b)).then_inc(acc_copied[1], 1)
                add_rows(1, b)
                row_stats(1, b)

            dve.wait_ge(g_ok[0], NB)
            newton(0, 0)
            newton(0, 1)
            mask(0, 0)
            with dve.Fori(1, NB) as b:
                newton(b, 0)
                mask(b - 1, 1)
                newton(b, 1)
                end_block1(b - 1)
                mask(b, 0)
            mask(NB - 1, 1)
            end_block1(NB - 1)

            def logits(g, s):
                r = g * BT + s
                row = A_flat[:, N * s:N * (s + 1)]
                dve.wait_ge(row_in[s], g * 16 + 16)
                dve.wait_ge(mx_ok, r)
                nc.vector.tensor_scalar(pen, row, 0.0, -BIG, ALU.is_le, ALU.mult).then_inc(pen_ok, 1)
                dve.wait_ge(pen_ok, r + 1)
                nc.vector.scalar_tensor_tensor(row, f2_bc[:, :], f1_col[:, bass.ds(r, 1)], row,
                                               ALU.add, ALU.mult).then_inc(t_ok, 1)
                hold(dve, (t_ok, r + 1))
                nc.vector.tensor_tensor_reduce(out=row, in0=row, in1=pen, scale=1.0, scalar=-3.0e38,
                                               op0=ALU.add, op1=ALU.max,
                                               accum_out=mx[:, s:s + 1]).then_inc(mx_ok, 1)
                dve.wait_ge(mx_ok, r + 1)
                nc.vector.tensor_scalar(negmx[:, s:s + 1], mx[:, s:s + 1], -1.0, None, ALU.mult).then_inc(nm_a, 1)
                nc.vector.scalar_tensor_tensor(row, row, SLOPE2, row, ALU.mult, ALU.max)
                dve.wait_ge(nm_a, r + 1)
                nc.vector.scalar_tensor_tensor(nm[:, s:s + 1], mx[:, s:s + 1], -SLOPE2, negmx[:, s:s + 1],
                                               ALU.mult, ALU.min).then_inc(l_ok, 1)

            def add_attention(b):
                hold(dve, (p_ok, b * BT + BT))
                nc.vector.reciprocal(rinv4, rsum[:, bass.ds(b * BT, BT)]).then_inc(rinv_ok, 1)
                dve.wait_ge(rinv_ok, b + 1)
                dve.wait_ge(y_rows[2], b + 1)
                for k in range(BT):
                    t = bass.ds(b * BT + k, 1)
                    op = nc.vector.scalar_tensor_tensor(X[:, t, :], epi_k[:, k:k + 1, :], rinv4[:, k:k + 1],
                                                        X[:, t, :], ALU.mult, ALU.add)
                op.then_inc(x_new[2], 1)
                row_stats(2, b)

            def table4(b):
                hold(dve, (g_mm[2], b + 1))
                nc.vector.tensor_copy(hs_flat, epi2).then_inc(g4_st, 1)

            for s in range(BT):
                logits(0, s)
            with dve.Fori(1, NB) as g:
                for s in range(BT):
                    logits(g, s)
                    if s == 2:
                        add_attention(g - 1)
                table4(g - 1)
            add_attention(NB - 1)
            table4(NB - 1)

            dve.wait_ge(l3_const, 4)
            with dve.Fori(0, NB) as b:
                dve.wait_ge(dbc_mm, b)
                for k in range(BT):
                    op = nc.vector.tensor_scalar(dg[:, k, :], ident[:, :], dinv[:, bass.ds(b * BT + k, 1)], None,
                                                 ALU.mult)
                op.then_inc(dg_ok, 1)
                dve.wait_ge(used[3], b * NC + NC)
                dve.wait_ge(sp_ok, b)
                dve.wait_ge(dbc_ok, b + 1)
                nc.vector.tensor_tensor(yT[:, :], acc(b), hs_flat, ALU.mult).then_inc(acc_copied[3], 1)
                dve.wait_ge(zb_ok, b + 1)
                nc.vector.scalar_tensor_tensor(block_cols(zT, b), zb, SLOPE3, zb, ALU.mult, ALU.max)\
                    .then_inc(z_ok, 1)
                dve.wait_ge(z_ok, b + 1)
                dve.wait_ge(sq_mm, b)
                nc.vector.tensor_tensor(zz, block_cols(zT, b), block_cols(zT, b), ALU.mult).then_inc(zz_ok, 1)
                hold(dve, (sq_mm, b + 1))
                nc.vector.tensor_copy(sq_col[:, bass.ds(b * BT, BT)], epi2[:, 0:BT]).then_inc(sqc_ok, 1)
                dve.wait_ge(sq_half, b + 1)
                nc.vector.tensor_copy(p1f, yT[:, :]).then_inc(sp_ch, 1)
                dve.wait_ge(sp_ch, b * 4 + 1)
                nc.vector.tensor_tensor(s2f, yT[:, :], p1f, ALU.subtract).then_inc(sp_ch, 1)
                dve.wait_ge(sp_ch, b * 4 + 2)
                nc.vector.tensor_copy(p2f, s2f).then_inc(sp_ch, 1)
                dve.wait_ge(sp_ch, b * 4 + 3)
                nc.vector.tensor_tensor(s3f, s2f, p2f, ALU.subtract).then_inc(sp_ch, 1)
                hold(dve, (sp_ch, b * 4 + 4))
                nc.vector.tensor_copy(block_cols(sq_parts[0:32, :], b), p1f[0:32, :])
                nc.vector.tensor_copy(block_cols(sq_parts[32:64, :], b), p2f[32:64, :])
                nc.vector.tensor_copy(block_cols(sq_parts[64:96, :], b), s3f[64:96, :]).then_inc(sp_ok, 1)

            with dve.Fori(0, NT // 2) as i:
                for u in range(2):
                    r = 2 * i + u
                    hold(dve, (key_ok, 2 * r + 2), (top_ok, r))
                    nc.vector.max(v8[u], keys[u]).then_inc(v8_ok, 1)
                    hold(dve, (v8_ok, r + 1))
                    nc.vector.max_index(i8[u], v8[u], keys[u]).then_inc(i8_ok, 1)
                    hold(dve, (i8_ok, r + 1))
                    nc.vector.tensor_copy(kval[:, bass.ds(r, 1), :], v8[u].unsqueeze(1))
                    nc.vector.tensor_copy(kidx[:, bass.ds(r, 1), :], i8[u].unsqueeze(1)).then_inc(top_ok, 1)

            dve.wait_ge(top_ok, NT)
            nc.vector.scalar_tensor_tensor(dist, kval[:, :, 0:TOP], -2.0,
                                           sq_col.unsqueeze(2).broadcast_to([P, NT, TOP]),
                                           ALU.mult, ALU.add).then_inc(d_ch, 1)
            dve.wait_ge(d_ch, 1)
            nc.vector.tensor_scalar(dist, dist, 0.0, 1e-10, ALU.max, ALU.add).then_inc(d_ch, 1)
            dve.wait_ge(s4_ok, 1)
            nc.vector.tensor_reduce(s4sum, S4, AX.X, ALU.add).then_inc(d_ch, 1)
            dve.wait_ge(d_ch, 3)
            nc.vector.tensor_tensor(s4sum, s4sum, deg, ALU.add).then_inc(d_ch, 1)
            dve.wait_ge(d2_ok, 1)
            dve.wait_ge(g4_in, 16)
            for c in range(NC):
                g = Ga[:, CT * c:CT * (c + 1), :]
                nc.vector.tensor_tensor(g, g, dinv2[:, CT * c:CT * (c + 1)].unsqueeze(2).broadcast_to([P, CT, P]),
                                        ALU.mult).then_inc(g4s_ok, 1)

            dve.wait_ge(xb_ok, 1)
            with dve.Fori(0, NB) as b:
                for s in range(BT):
                    u, r = s % 2, b * BT + s
                    dst = gsum[:, bass.ds(r, 1), :]
                    dve.wait_ge(gath_in[u], b * (2 * 64) + 64 * (s // 2 + 1))
                    for k in range(TOP):
                        w = S4[:, bass.ds(r, 1), k:k + 1].rearrange("p a b -> p (a b)")
                        src = gath[u][:, k:k + 1, :]
                        if k == 0:
                            op = nc.vector.tensor_scalar(dst, src, w, None, ALU.mult)
                        else:
                            dve.wait_ge(gs_ch, r * TOP + k)
                            op = nc.vector.scalar_tensor_tensor(dst, src, w, dst, ALU.mult, ALU.add)
                        op.then_inc(gs_ch, 1)
                dve.wait_ge(gs_ch, b * (BT * TOP) + BT * TOP)
                dve.wait_ge(y_rows[4], b + 1)
                nc.vector.tensor_tensor(hs[:, :, :], epi_k, rows(gsum, b), ALU.add).then_inc(o_sum, 1)
                dve.wait_ge(o_sum, b + 1)
                for k in range(BT):
                    t = bass.ds(b * BT + k, 1)
                    op = nc.vector.scalar_tensor_tensor(X[:, t, :], hs[:, k:k + 1, :], dinv2[:, t], X[:, t, :],
                                                        ALU.mult, ALU.add)
                op.then_inc(o_ok, 1)

        @block.gpsimd
        def _(pool):
            nc.gpsimd.memset(ident[:, :], 0.0).then_inc(consts, 1)
            pool.wait_ge(consts, 1)
            nc.gpsimd.affine_select(out=ident[:, :], in_=ident[:, :], compare_op=ALU.not_equal, fill=1.0,
                                    base=0, pattern=[[-1, P]], channel_multiplier=1).then_inc(consts, 1)
            nc.gpsimd.memset(one_c, 1.0)
            nc.gpsimd.memset(mhalf_c, -0.5)
            nc.gpsimd.memset(half_c, 0.5)
            nc.gpsimd.memset(tiny_c, TINY).then_inc(consts, 1)
            pool.wait_ge(consts, 3)
            pool.wait_ge(s_stat, 6)
            nc.gpsimd.tensor_scalar(var0, var0, EPS, None, ALU.add).then_inc(s_pool, 1)
            pool.wait_ge(s_pool, 1)
            nc.gpsimd.tensor_tensor(rstd0, var0, mhalf_c.broadcast_to([P, NT]), ALU.pow).then_inc(s_pool, 1)
            pool.wait_ge(s_pool, 2)
            nc.gpsimd.tensor_tensor(nmr0, mean0, rstd0, ALU.mult).then_inc(s_pool, 1)
            pool.wait_ge(s_pool, 3)
            nc.gpsimd.tensor_scalar(nmr0, nmr0, -1.0, None, ALU.mult).then_inc(s_rstd, 1)

            def block_rstd(L, b):
                hold(pool, (stats[L], b + 1))
                nc.gpsimd.tensor_scalar(ve4, mv4[:, :, 1], EPS, None, ALU.add).then_inc(pool_ch[L], 1)
                pool.wait_ge(pool_ch[L], b * 3 + 1)
                nc.gpsimd.tensor_tensor(rstd4, ve4, mhalf_c.broadcast_to([P, BT]), ALU.pow).then_inc(pool_ch[L], 1)
                pool.wait_ge(pool_ch[L], b * 3 + 2)
                nc.gpsimd.tensor_tensor(nmr4, mv4[:, :, 0], rstd4, ALU.mult).then_inc(pool_ch[L], 1)
                hold(pool, (pool_ch[L], b * 3 + 3))
                nc.gpsimd.tensor_scalar(nmr4, nmr4, -1.0, None, ALU.mult).then_inc(rstd_ok[L], 1)

            with pool.Fori(0, NB) as b:
                block_rstd(0, b)
            pool.wait_ge(deg_ok, NB)
            nc.gpsimd.tensor_tensor(dinv, deg, mhalf_c.broadcast_to([P, NT]), ALU.pow).then_inc(dinv_ok, 1)
            with pool.Fori(0, NB) as b:
                block_rstd(1, b)
            with pool.Fori(0, NB) as b:
                block_rstd(2, b)
                hold(pool, (g4_st, b + 1))
                nc.gpsimd.dma_start(table4_rows[:, bass.ds(b * BT, BT), :], hs[:, :, :]).then_inc(g4_out, 16)

            pool.wait_ge(m_done, 2 * NB)
            nc.gpsimd.memset(ones, 1.0)
            nc.gpsimd.memset(sq_parts, 0.0)
            nc.gpsimd.memset(pick, 0.0).then_inc(l3_const, 1)
            pool.wait_ge(l3_const, 1)
            for part in range(3):
                nc.gpsimd.memset(pick[32 * part:32 * part + 1, :], 1.0).then_inc(l3_const, 1)
            pool.wait_ge(l3_const, 4)
            nc.gpsimd.dma_start(b32_bc, b32.partition_broadcast(P)).then_inc(b32_in, 16)
            pool.wait_ge(g4_out, 16 * NB)
            nc.gpsimd.dma_start(Ga[:, :, :], table4_rows).then_inc(g4_in, 16)
            pool.wait_ge(h_rows[2], NB)
            pool.wait_ge(b32_in, 16)
            nc.gpsimd.tensor_tensor(X[:, :, :], X[:, :, :], b32_bc.unsqueeze(1).broadcast_to([P, NT, P]),
                                    ALU.add).then_inc(xb_ok, 1)
            pool.wait_ge(z_ok, NB)

            def stage_z(r, u):
                if not isinstance(r, int):
                    hold(pool, (key_mm, 2 * r - 2))
                nc.gpsimd.tensor_copy(z_st[u], zT[:, r * P:(r + 1) * P] if isinstance(r, int)
                                      else zT[:, bass.ds(r * P, P)]).then_inc(zst_ok, 1)

            stage_z(0, 0)
            stage_z(1, 1)
            with pool.Fori(1, NT // 2) as i:
                stage_z(2 * i, 0)
                stage_z(2 * i + 1, 1)
            pool.wait_ge(d_ch, 2)
            nc.gpsimd.tensor_tensor(dist, dist, half_c.unsqueeze(2).broadcast_to([P, NT, TOP]), ALU.pow)\
                .then_inc(d_pool, 1)
            pool.wait_ge(d_ch, 4)
            nc.gpsimd.tensor_tensor(dinv2, s4sum, mhalf_c.broadcast_to([P, NT]), ALU.pow).then_inc(d2_ok, 1)
            pool.wait_ge(g4s_ok, NC)
            nc.gpsimd.dma_start(table4s_rows, Ga[:, :, :]).then_inc(g4s_out, 16)
            pool.wait_ge(g4s_out, 16)
            with pool.Fori(0, NT // 2) as i:
                for u in range(2):
                    r = 2 * i + u
                    hold(pool, (gs_ch, i * (2 * TOP)))
                    nc.gpsimd.tensor_copy(idx_st[u], kidx[:, bass.ds(r, 1), 0:TOP].rearrange("p a b -> p (a b)"))\
                        .then_inc(idx_ok, 1)
                    hold(pool, (idx_ok, r + 1))
                    for k in range(TOP):
                        nc.gpsimd.indirect_dma_start(
                            gath[u][:, k, :], None, table4s_dram,
                            bass.IndirectOffsetOnAxis(ap=idx_st[u][:, k:k + 1], axis=0)).then_inc(gath_in[u], 16)


_OUT = ((N, P), "float32")


def kernel(x, adj, L0_gnn_W, L0_gnn_b, L1_gnn_W, L1_gnn_B, L1_gnn_mu, L1_gnn_sigma, L2_gnn_inlayer2,
           L2_gnn_W1, L2_gnn_w2, L2_gnn_b2, L2_gnn_w3, L2_gnn_b3, L3_gnn_W1, L3_gnn_b1, L3_gnn_W2, L3_gnn_b2):
    import numpy as _np
    import concourse.bacc as _bacc
    from concourse import mybir as _mybir
    from concourse.bass_utils import run_bass_kernel_spmd as _run

    def t(a):
        return _np.asarray(a).T

    host = {
        "x": x, "adj": adj, "adjT": t(adj), "w0T": t(L0_gnn_W), "b0": L0_gnn_b, "w1": L1_gnn_W,
        "b1": L1_gnn_B, "mu": L1_gnn_mu, "sigma": L1_gnn_sigma, "inlT": t(L2_gnn_inlayer2),
        "wfT": t(L2_gnn_W1), "wf1": L2_gnn_w2, "bf1": _np.reshape(L2_gnn_b2, (1,)), "wf2": L2_gnn_w3,
        "bf2": _np.reshape(L2_gnn_b3, (1,)), "w31": L3_gnn_W1, "b31": L3_gnn_b1, "w32": L3_gnn_W2,
        "b32": L3_gnn_b2,
    }
    nc = _bacc.Bacc("TRN2", target_bir_lowering=False, num_devices=1)
    arrays, args = {}, []
    for name, value in host.items():
        a = _np.ascontiguousarray(value)
        arrays[f"in_{name}"] = a
        args.append(nc.dram_tensor(f"in_{name}", a.shape, _mybir.dt.from_np(a.dtype), kind="ExternalInput").ap())
    shape, dtype = _OUT
    args.append(nc.dram_tensor("out_0", shape, _mybir.dt.from_np(_np.dtype(dtype)), kind="ExternalOutput").ap())
    gnn_kernel(nc, *args)
    r = _run(nc, [arrays], core_ids=[0])
    return r.results[0]["out_0"]
```
